# Optimizing a Trainium2 kernel written in Bass

```python
import numpy as np
import jax
import jax.numpy as jnp

def _softmax(x, axis=-1):
    return jax.nn.softmax(x, axis=axis)

def _gelu(x):
    return jax.nn.gelu(x, approximate=True)

def _silu(x):
    return jax.nn.silu(x)

def _sigmoid(x):
    return jax.nn.sigmoid(x)

def _layernorm(x, axis=-1, eps=1e-05):
    m = jnp.mean(x, axis=axis, keepdims=True)
    v = jnp.var(x, axis=axis, keepdims=True)
    return (x - m) / jnp.sqrt(v + eps)

def _scatter_add(tgt, idx, src, axis=0):
    return tgt.at[idx].add(src)

def _segment_sum(src, seg, n):
    return jax.ops.segment_sum(src, seg, n)
kernel_name = 'mk_gnn_ffn_d2_gnn_r8_be680a'

def setup_inputs(seed: int=0):
    np.random.seed(seed)
    _w = jnp.asarray

    def _rec_inputs():
        import jax
        import jax.numpy as jnp
        _gk = jax.random.key(seed)
        x = -0.0003713 + 1 * jax.random.normal(jax.random.fold_in(_gk, 1), (12500, 256), jnp.float32)
        src = jax.random.randint(jax.random.fold_in(_gk, 2), (200000,), 0, 12500, jnp.int32)
        dst = jnp.minimum((12500 * jax.random.uniform(jax.random.fold_in(_gk, 3), (200000,)) ** 2.0).astype(jnp.int32), 99999)
        _o = jnp.argsort(dst, stable=True)
        src = src[_o]
        dst = dst[_o]
        edge_type_16 = jax.random.randint(jax.random.fold_in(_gk, 12), (200000,), 0, 16, jnp.int32)
        edge_weight1 = jax.random.uniform(jax.random.fold_in(_gk, 13), (200000, 1), jnp.float32, 0.0, 1)
        return (x, src, dst, edge_type_16, edge_weight1)
    x, src, dst, edge_type_16, edge_weight1 = _rec_inputs()

    def _L0_gnn_setup():
        import jax, jax.numpy as jnp
        import numpy as np
        N_NODES = 6250
        key = jax.random.key(seed)
        k1, k2, k3, k4, k5, k6 = jax.random.split(key, 6)
        N, E, DIN, DOUT = (N_NODES, 100000, 256, 256)
        h = jax.random.normal(k1, (N, DIN), dtype=jnp.float32)
        e_w = jax.random.uniform(k2, (E, 1), dtype=jnp.float32)
        src = jax.random.randint(k3, (E,), 0, N, dtype=jnp.int32)
        dst = jax.random.randint(k4, (E,), 0, N, dtype=jnp.int32)
        stdv = 1.0 / np.sqrt(DOUT)
        weight = jax.random.uniform(k5, (DIN, DOUT), dtype=jnp.float32, minval=-stdv, maxval=stdv)
        bias = jax.random.uniform(k6, (DOUT,), dtype=jnp.float32, minval=-stdv, maxval=stdv)
        return {'h': h, 'e_w': e_w, 'src': src, 'dst': dst, 'weight': weight, 'bias': bias}
    _L0_gnn_all = _L0_gnn_setup()
    _L0_gnn_in = {k: v for k, v in _L0_gnn_all.items() if k in ('weight', 'bias')}
    del _L0_gnn_all

    def _L0_ffn_setup():
        import jax, jax.numpy as jnp
        import numpy as np
        NUM_EXPERTS = 8
        TOP_K = 2
        B, S, D = (8, 1024, 256)

        def _moe(tokens, router_w, w1, b1, w2, b2):
            N = tokens.shape[0]
            E = router_w.shape[0]
            logits = tokens.astype(jnp.float32) @ router_w.astype(jnp.float32).T
            probs = jax.nn.softmax(logits, axis=-1)
            rw, re = jax.lax.top_k(probs, TOP_K)
            if TOP_K > 1:
                rw = rw / jnp.maximum(rw.sum(-1, keepdims=True), 1e-12)
            rw = rw.astype(tokens.dtype)
            combine = jnp.zeros((N, E), tokens.dtype).at[jnp.arange(N)[:, None], re].set(rw)
            out = tokens
            for e in range(E):
                h = jax.nn.gelu(tokens @ w1[e] + b1[e], approximate=False)
                y = h @ w2[e] + b2[e]
                out = out + combine[:, e:e + 1] * y
            return out
        key = jax.random.key(seed)
        ks = jax.random.split(key, 4)
        scale = 1.0 / np.sqrt(D).astype(np.float32)
        return {'input_embeddings': jax.random.normal(ks[0], (B, S, D), jnp.float32), 'router_w': jax.random.normal(ks[1], (NUM_EXPERTS, D), jnp.float32) * scale, 'w1': jax.random.normal(ks[2], (NUM_EXPERTS, D, D), jnp.float32) * scale, 'b1': jnp.zeros((NUM_EXPERTS, D), jnp.float32), 'w2': jax.random.normal(ks[3], (NUM_EXPERTS, D, D), jnp.float32) * scale, 'b2': jnp.zeros((NUM_EXPERTS, D), jnp.float32)}
    _L0_ffn_all = _L0_ffn_setup()
    _L0_ffn_in = {k: v for k, v in _L0_ffn_all.items() if k in ('router_w', 'w1', 'b1', 'w2', 'b2')}
    del _L0_ffn_all

    def _L1_gnn_setup():
        import jax, jax.numpy as jnp
        import numpy as np
        N_NODES = 6250
        N_EDGES = 100000
        HDIM = 256
        NUMRELS = 16

        def _gru_cell(x, h, w_ih, w_hh, b_ih, b_hh):
            gi = x @ w_ih.T + b_ih
            gh = h @ w_hh.T + b_hh
            i_r, i_z, i_n = jnp.split(gi, 3, axis=-1)
            h_r, h_z, h_n = jnp.split(gh, 3, axis=-1)
            r = jax.nn.sigmoid(i_r + h_r)
            z = jax.nn.sigmoid(i_z + h_z)
            n = jnp.tanh(i_n + r * h_n)
            return (1.0 - z) * n + z * h
        key = jax.random.key(seed)
        ks = jax.random.split(key, 9)
        h = jax.random.normal(ks[0], (N_NODES, HDIM), dtype=jnp.float32)
        relvectors = jax.random.normal(ks[1], (NUMRELS, HDIM), dtype=jnp.float32)
        s = 1.0 / np.sqrt(HDIM)
        w_ih = jax.random.uniform(ks[2], (3 * HDIM, HDIM), minval=-s, maxval=s, dtype=jnp.float32)
        w_hh = jax.random.uniform(ks[3], (3 * HDIM, HDIM), minval=-s, maxval=s, dtype=jnp.float32)
        b_ih = jax.random.uniform(ks[4], (3 * HDIM,), minval=-s, maxval=s, dtype=jnp.float32)
        b_hh = jax.random.uniform(ks[5], (3 * HDIM,), minval=-s, maxval=s, dtype=jnp.float32)
        edge_src = jax.random.randint(ks[6], (N_EDGES,), 0, N_NODES, dtype=jnp.int32)
        edge_dst = jax.random.randint(ks[7], (N_EDGES,), 0, N_NODES, dtype=jnp.int32)
        edge_rel = jax.random.randint(ks[8], (N_EDGES,), 0, NUMRELS, dtype=jnp.int32)
        return {'h': h, 'relvectors': relvectors, 'w_ih': w_ih, 'w_hh': w_hh, 'b_ih': b_ih, 'b_hh': b_hh, 'edge_src': edge_src, 'edge_dst': edge_dst, 'edge_rel': edge_rel}
    _L1_gnn_all = _L1_gnn_setup()
    _L1_gnn_in = {k: v for k, v in _L1_gnn_all.items() if k in ('relvectors', 'w_ih', 'w_hh', 'b_ih', 'b_hh')}
    del _L1_gnn_all

    def _L1_ffn_setup():
        import math
        import jax, jax.numpy as jnp
        import numpy as np
        CAPACITY_FACTOR = 1.25
        key = jax.random.key(seed)
        ks = jax.random.split(key, 5)
        B, L, D, F, E = (8, 1024, 256, 1024, 8)
        h = jax.random.normal(ks[0], (B, L, D), dtype=jnp.float32)
        gate_w = jax.random.normal(ks[1], (D, E), dtype=jnp.float32) * 0.02
        gate_b = jnp.zeros((E,), dtype=jnp.float32)
        w1 = jax.random.normal(ks[2], (E, D, F), dtype=jnp.float32) * (1.0 / math.sqrt(D))
        b1 = jnp.zeros((E, F), dtype=jnp.float32)
        w2 = jax.random.normal(ks[3], (E, F, D), dtype=jnp.float32) * (1.0 / math.sqrt(F))
        b2 = jnp.zeros((E, D), dtype=jnp.float32)
        return {'h': h, 'gate_w': gate_w, 'gate_b': gate_b, 'w1': w1, 'b1': b1, 'w2': w2, 'b2': b2}
    _L1_ffn_all = _L1_ffn_setup()
    _L1_ffn_in = {k: v for k, v in _L1_ffn_all.items() if k in ('gate_w', 'gate_b', 'w1', 'b1', 'w2', 'b2')}
    del _L1_ffn_all
    return {'x': x, 'src': src, 'dst': dst, 'edge_type_16': edge_type_16, 'edge_weight1': edge_weight1, 'L0_gnn_weight': _L0_gnn_in['weight'], 'L0_gnn_bias': _L0_gnn_in['bias'], 'L0_ffn_router_w': _L0_ffn_in['router_w'], 'L0_ffn_w1': _L0_ffn_in['w1'], 'L0_ffn_b1': _L0_ffn_in['b1'], 'L0_ffn_w2': _L0_ffn_in['w2'], 'L0_ffn_b2': _L0_ffn_in['b2'], 'L1_gnn_relvectors': _L1_gnn_in['relvectors'], 'L1_gnn_w_ih': _L1_gnn_in['w_ih'], 'L1_gnn_w_hh': _L1_gnn_in['w_hh'], 'L1_gnn_b_ih': _L1_gnn_in['b_ih'], 'L1_gnn_b_hh': _L1_gnn_in['b_hh'], 'L1_ffn_gate_w': _L1_ffn_in['gate_w'], 'L1_ffn_gate_b': _L1_ffn_in['gate_b'], 'L1_ffn_w1': _L1_ffn_in['w1'], 'L1_ffn_b1': _L1_ffn_in['b1'], 'L1_ffn_w2': _L1_ffn_in['w2'], 'L1_ffn_b2': _L1_ffn_in['b2']}

def reference(x, src, dst, edge_type_16, edge_weight1, L0_gnn_weight, L0_gnn_bias, L0_ffn_router_w, L0_ffn_w1, L0_ffn_b1, L0_ffn_w2, L0_ffn_b2, L1_gnn_relvectors, L1_gnn_w_ih, L1_gnn_w_hh, L1_gnn_b_ih, L1_gnn_b_hh, L1_ffn_gate_w, L1_ffn_gate_b, L1_ffn_w1, L1_ffn_b1, L1_ffn_w2, L1_ffn_b2):
    import jax
    import jax.numpy as jnp

    def _L0_gnn_ref(h, e_w, src, dst, weight, bias):
        import jax, jax.numpy as jnp
        import numpy as np
        N_NODES = 6250
        m = h[src] * e_w
        agg = jax.ops.segment_sum(m, dst, num_segments=h.shape[0])
        return agg @ weight + bias

    def _L0_ffn_ref(input_embeddings, router_w, w1, b1, w2, b2):
        import jax, jax.numpy as jnp
        import numpy as np
        NUM_EXPERTS = 8
        TOP_K = 2
        B, S, D = (8, 1024, 256)

        def _moe(tokens, router_w, w1, b1, w2, b2):
            N = tokens.shape[0]
            E = router_w.shape[0]
            logits = tokens.astype(jnp.float32) @ router_w.astype(jnp.float32).T
            probs = jax.nn.softmax(logits, axis=-1)
            rw, re = jax.lax.top_k(probs, TOP_K)
            if TOP_K > 1:
                rw = rw / jnp.maximum(rw.sum(-1, keepdims=True), 1e-12)
            rw = rw.astype(tokens.dtype)
            combine = jnp.zeros((N, E), tokens.dtype).at[jnp.arange(N)[:, None], re].set(rw)
            out = tokens
            for e in range(E):
                h = jax.nn.gelu(tokens @ w1[e] + b1[e], approximate=False)
                y = h @ w2[e] + b2[e]
                out = out + combine[:, e:e + 1] * y
            return out
        b, s, d = input_embeddings.shape
        tokens = input_embeddings.reshape(b * s, d)
        return _moe(tokens, router_w, w1, b1, w2, b2).reshape(b, s, d)

    def _L1_gnn_ref(h, relvectors, w_ih, w_hh, b_ih, b_hh, edge_src, edge_dst, edge_rel):
        import jax, jax.numpy as jnp
        import numpy as np
        N_NODES = 6250
        N_EDGES = 100000
        HDIM = 256
        NUMRELS = 16

        def _gru_cell(x, h, w_ih, w_hh, b_ih, b_hh):
            gi = x @ w_ih.T + b_ih
            gh = h @ w_hh.T + b_hh
            i_r, i_z, i_n = jnp.split(gi, 3, axis=-1)
            h_r, h_z, h_n = jnp.split(gh, 3, axis=-1)
            r = jax.nn.sigmoid(i_r + h_r)
            z = jax.nn.sigmoid(i_z + h_z)
            n = jnp.tanh(i_n + r * h_n)
            return (1.0 - z) * n + z * h
        msg = h[edge_src] + relvectors[edge_rel]
        red = jax.ops.segment_sum(msg, edge_dst, num_segments=h.shape[0])
        return _gru_cell(red, h, w_ih, w_hh, b_ih, b_hh)

    def _L1_ffn_ref(h, gate_w, gate_b, w1, b1, w2, b2):
        import math
        import jax, jax.numpy as jnp
        import numpy as np
        CAPACITY_FACTOR = 1.25
        B, L, D = h.shape
        E = gate_w.shape[1]
        T = B * L
        C = max(1, math.ceil(CAPACITY_FACTOR * T / E))
        x = h.reshape(T, D)
        logits = x @ gate_w + gate_b
        probs = jax.nn.softmax(logits, axis=-1)
        idx = jnp.argmax(probs, axis=-1)
        prb = jnp.take_along_axis(probs, idx[:, None], axis=1)[:, 0]
        one_hot = jax.nn.one_hot(idx, E, dtype=jnp.float32)
        pos = (jnp.cumsum(one_hot, axis=0) * one_hot).sum(-1).astype(jnp.int32) - 1
        kept = pos < C
        pos_safe = jnp.where(kept, pos, C)
        buf = jnp.zeros((E, C, D), dtype=h.dtype).at[idx, pos_safe].set(x, mode='drop')
        hmid = jax.nn.relu(jnp.einsum('ecd,edf->ecf', buf, w1) + b1[:, None, :])
        ybuf = jnp.einsum('ecf,efd->ecd', hmid, w2) + b2[:, None, :]
        pos_g = jnp.minimum(pos, C - 1)
        y_tok = ybuf[idx, pos_g] * (prb * kept)[:, None]
        y = y_tok.reshape(B, L, D)
        y = jnp.nan_to_num(y, nan=0.0, posinf=10000.0, neginf=-10000.0)
        return y
    x = x + _L0_gnn_ref(_layernorm(x, axis=-1), edge_weight1, src, dst, L0_gnn_weight, L0_gnn_bias)
    x = x + _L0_ffn_ref(_layernorm(x, axis=-1)[None], L0_ffn_router_w, L0_ffn_w1, L0_ffn_b1, L0_ffn_w2, L0_ffn_b2)[0]
    x = x + _L1_gnn_ref(_layernorm(x, axis=-1), L1_gnn_relvectors, L1_gnn_w_ih, L1_gnn_w_hh, L1_gnn_b_ih, L1_gnn_b_hh, src, dst, edge_type_16)
    x = x + _L1_ffn_ref(_layernorm(x, axis=-1)[None], L1_ffn_gate_w, L1_ffn_gate_b, L1_ffn_w1, L1_ffn_b1, L1_ffn_w2, L1_ffn_b2)[0]
    return x

_drawn_inputs = setup_inputs


def setup_inputs(seed=0):
    import zlib

    import numpy as np

    out = dict(_drawn_inputs(seed))
    spreads = {'L0_ffn_b1': (0.0, 0.381),
     'L0_ffn_b2': (0.0, 0.1),
     'L1_ffn_gate_b': (0.0, 0.351),
     'L1_ffn_b1': (0.0, 2.0),
     'L1_ffn_b2': (0.0, 0.8)}
    factors = {'L1_gnn_b_ih': 8.0, 'L1_gnn_b_hh': 8.0}
    for name, (base, spread) in spreads.items():
        noise = np.random.default_rng([zlib.crc32(name.encode()), seed]).standard_normal(out[name].shape)
        drawn = base * np.exp(spread * noise) if base else spread * noise
        out[name] = jnp.asarray(drawn.astype(out[name].dtype))
    for name, factor in factors.items():
        out[name] = (out[name] * factor).astype(out[name].dtype)
    return out
```

```python
from contextlib import ExitStack

import concourse.bass as bass
from concourse import mybir

P = 128
N, D, E = 12500, 256, 200000
NT = -(-N // P)
NPAIR = NT // 2
NPAD = NT * P
LAST = N - (NT - 1) * P
RT = 16
RC = RT // 2
T = -(-(-(-E // P)) // RT) * RT
NCH = T // 2
EPAD = T * P
FP, FK = 112, NCH // 112
FAR = 1 << 20
NREL = 16
RW = D + NREL
NE0, NE1, F1 = 8, 8, 1024
KD, KF = D // P, F1 // P
CAP = -(-5 * N // (4 * NE1))
XCH, XT = 7, NT // 7
GROUPS = 4
STILES = NE1 * GROUPS * 4
EPS = 1e-5
BIG = 3.4028234663852886e38


def build(nc, a):
    f32, i32, u32 = mybir.dt.float32, mybir.dt.int32, mybir.dt.uint32
    ALU, ACT, AX = mybir.AluOpType, mybir.ActivationFunctionType, mybir.AxisListType
    ds = bass.ds
    ctx = ExitStack()
    with ctx:
        def sb(name, shape, dt=f32):
            return ctx.enter_context(nc.sbuf_tensor(name, shape, dt))

        def sem(name):
            return ctx.enter_context(nc.semaphore(name))

        hw_d = nc.dram_tensor("hw_rows", (NPAD, D), f32).ap()
        h1_d = nc.dram_tensor("h1_rows", (NPAD, D), f32).ap()
        x3_d = nc.dram_tensor("x3_rows", (NPAD, D), f32).ap()
        rows = [d.rearrange("(n p) f -> p n f", p=P) for d in (hw_d, h1_d, x3_d)]
        hw_t, h1_t, x3_t = rows

        xs = sb("xs", [P, NT * D])
        ring = sb("ring", [P, RT * RW])
        srcs = sb("srcs", [P, T], i32)
        dsts = sb("dsts", [P, 2 + T])
        wts = sb("wts", [P, T])
        rels = sb("rels", [P, T])
        wide = sb("wide", [P, 9216])
        ident = sb("ident", [P, P])
        ones = sb("ones", [P, P])
        upper = sb("upper", [P, P])
        iota0 = sb("iota0", [P, P])
        iota = sb("iota", [P, P])
        rel_iota = sb("rel_iota", [P, NREL])
        sched = sb("sched", [1, 4 * P], i32)
        idxs = sb("idxs", [P, RT], i32)
        S = [sb(f"onehot{j}", [P, P]) for j in range(2)]
        tn = sb("tn", [P, 2 * D])
        tT = sb("tT", [P, 2 * D])
        pairo = sb("pairo", [P, 2 * D])
        st = sb("st", [P, 4 * 6])
        mean, var, rstd, nt1 = sb("mean", [P, 4]), sb("var", [P, 4]), sb("rstd", [P, 4]), sb("nt1", [P, 4])
        small = sb("small", [P, 256])
        smalli = sb("smalli", [P, 64], u32)
        invt = sb("invt", [P, 2 * P])
        tok1 = sb("tok1", [P, 2])

        hT = [sb(f"hT{j}", [P, 2 * D]) for j in range(2)]

        w1_0 = wide[:, 0:4096]
        w2_0 = wide[:, 4096:8192]
        wg = wide[:, 8192:8704]
        rwT = sb("rwT", [P, KD * NE0])
        b1_0 = sb("b1_0", [P, NE0 * 2])
        b2_0 = sb("b2_0", [NE0, D])
        gbias = sb("gbias", [P, D])
        combT = sb("combT", [NE0, 2 * P])
        wih, whh = wide[:, 0:1536], wide[:, 1536:3072]
        relw = wide[0:17, 3072:4096]
        gates = [wide[:, 4096 + 512 * t:4608 + 512 * t] for t in range(2)]
        gn = [wide[:, 5120 + 256 * t:5376 + 256 * t] for t in range(2)]
        ga = [wide[:, 5632 + 256 * t:5888 + 256 * t] for t in range(2)]
        gT = [wide[:, 6144 + 512 * t:6656 + 512 * t] for t in range(2)]
        red = [wide[:, 7168 + 273 * t:7441 + 273 * t] for t in range(2)]
        cT = [wide[0:17, 7714 + 128 * t:7842 + 128 * t] for t in range(2)]
        hin = wide[:, 7970:8482]
        relT = wide[:, 8482:8482 + 2 * 17]
        brow = wide[0:1, 8520:8520 + 1]
        ohlo = [hT[0][:, 128 * t:128 * t + 128] for t in range(2)]
        ohhi = [hT[1][:, 256 * t:256 * t + 256] for t in range(2)]
        gateT = sb("gateT", [P, KD * NE1])
        gateb = sb("gateb", [1, NE1])
        bih, bhh = sb("bih", [1, 3 * D]), sb("bhh", [1, 3 * D])
        e16 = sb("e16", [1, 17])
        ohs = sb("ohs", [P, 3 * NE1])
        we1 = [xs[:, 4096 * b:4096 * b + 2048] for b in range(2)]
        we2 = [xs[:, 4096 * b + 2048:4096 * b + 4096] for b in range(2)]
        be2 = [xs[:, 8192 + 256 * b:8448 + 256 * b] for b in range(2)]
        be1 = xs[:, 8704:8704 + NE1 * KF]
        xg = [xs[:, 8768 + 1024 * b:9792 + 1024 * b] for b in range(2)]
        xn = xs[:, 10816:11840]
        xT = xs[:, 11840:12864]
        hE = xs[:, 12864:16960]
        yo = [xs[:, 16960 + 1024 * b:17984 + 1024 * b] for b in range(2)]
        ya = xs[:, 19008:19264]
        c1e4, cm1e4 = xs[:, 19264:19520], xs[:, 19520:19776]
        gidx = xs[:, 19776:19784].bitcast(i32)
        sidx = xs[:, 19784:19792].bitcast(i32)
        tokg = xs[:, 19792:19920].bitcast(i32)
        toks = xs[:, 19920:20048].bitcast(i32)
        yz = xs[:, 20048:20304]
        ym = xs[:, 20304:20560].bitcast(i32)

        bank = [ctx.enter_context(nc.psum_tensor(f"bank{k}", [P, 512], f32)) for k in range(8)]
        agg = bank[0:2]

        consts_made, tables_in, weights0_in = sem("consts_made"), sem("tables_in"), sem("weights0_in")
        x_in = [sem(f"x_in{c}") for c in range(XCH + 1)]
        x_cleared, x_chunks, sched_made = sem("x_cleared"), sem("x_chunks"), sem("sched_made")
        cnt_made, cnt_read = sem("cnt_made"), sem("cnt_read")
        tables_f = sem("tables_f")
        p_tn, p_tr, p_tT, p_mm, p_out, p_st, x_biased = (sem("p_" + n) for n in
                                                         ("tn", "tr", "tT", "mm", "out", "st", "bias"))
        passed = sem("passed")
        hw_stored, ring_clear = sem("hw_stored"), sem("ring_clear")

        class Layer:
            def __init__(self, n):
                self.slot = [sem(f"slot{n}_{k}") for k in range(RT)]
                self.landed, self.ring_free = sem(f"landed{n}"), sem(f"ring_free{n}")
                self.idx_set = sem(f"idx_set{n}")
                self.made = [sem(f"made{n}_{j}") for j in range(2)]
                self.used = [sem(f"used{n}_{j}") for j in range(2)]
                self.agg_ready, self.agg_free = sem(f"agg_ready{n}"), sem(f"agg_free{n}")
                self.rows = hw_d if n == 0 else h1_d

        L0, L1 = Layer(0), Layer(1)
        t_ready, t_tr, tT_ready, lg_ready, ls_ready, ex_ready = (sem("f_" + n) for n in
            ("t_ready", "t_tr", "tT_ready", "logits", "shifted", "exps"))
        comb_ready, combT_tr, combT_in = sem("comb_ready"), sem("combT_tr"), sem("combT_in")
        h_ready, gelu_done, mm2_done, acc_done = sem("h_ready"), sem("gelu_done"), sem("mm2_done"), sem("acc_done")
        h1_ready, h1_store, h1_stored = sem("h1_ready"), sem("h1_store"), sem("h1_stored")
        weights1_in, relw_mm, relw_in, l1_consts = sem("weights1_in"), sem("relw_mm"), sem("relw_in"), sem("l1_consts")
        hin_in = sem("hin_in")
        red_in, g_tr, g_T, g_mm, g_tanh = sem("red_in"), sem("g_tr"), sem("g_T"), sem("g_mm"), sem("g_tanh")
        g_pre, g_n, x3_ready, x3_store = sem("g_pre"), sem("g_n"), sem("x3_ready"), sem("x3_store")
        r_t, r_tr, r_T, r_lg, r_ls, r_ex = (sem("r_" + n) for n in ("t", "tr", "T", "lg", "ls", "ex"))
        r_oh, r_pos, r_slot, r_inv, r_done = (sem("r_" + n) for n in ("oh", "pos", "slot", "inv", "done"))
        x3_stored, e_consts = sem("x3_stored"), sem("e_consts")
        we_in = [sem(f"we_in{b}") for b in range(2)]
        be1_in, e_used = sem("be1_in"), sem("e_used")
        xg_in = [[sem(f"xg_in{b}_{t}") for t in range(4)] for b in range(2)]
        e_idx, e_issued, e_norm, e_tr, e_T, e_h, e_relu, e_y, e_out = (sem("e_" + n) for n in
            ("idx", "issued", "norm", "tr", "T", "h", "relu", "y", "out"))
        scat = [[sem(f"scat{b}_{t}") for t in range(4)] for b in range(2)]

        def hold(eng, sem_, value):
            eng.wait_ge(sem_, value)
            eng.sem_inc(passed, 1)

        def moments(v, st_, mean_, rstd_, var_, tmp_):
            s6 = st_.rearrange("p (n c) -> p n c", c=6)
            nc.vector.tensor_tensor(mean_, s6[:, :, 1], s6[:, :, 4], ALU.add)
            nc.vector.tensor_tensor(tmp_, s6[:, :, 1], s6[:, :, 4], ALU.subtract)
            nc.vector.tensor_tensor(var_, s6[:, :, 2], s6[:, :, 5], ALU.add)
            v.drain()
            nc.vector.tensor_scalar(mean_, mean_, 0.5, None, ALU.mult)
            nc.vector.scalar_tensor_tensor(out=tmp_, in0=tmp_, scalar=0.25, in1=tmp_, op0=ALU.mult, op1=ALU.mult)
            nc.vector.tensor_scalar(var_, var_, 1.0 / D, EPS, ALU.mult, ALU.add)
            v.drain()
            nc.vector.tensor_tensor(var_, var_, tmp_, ALU.add)
            v.drain()
            nc.vector.tensor_scalar(rstd_.bitcast(i32), var_.bitcast(i32), 1, None, ALU.logical_shift_right)
            v.drain()
            nc.vector.tensor_scalar(rstd_.bitcast(i32), rstd_.bitcast(i32), -1.0, float(0x5F3759DF), ALU.mult, ALU.add)
            for _ in range(3):
                v.drain()
                nc.vector.tensor_tensor(tmp_, rstd_, rstd_, ALU.mult)
                v.drain()
                nc.vector.tensor_tensor(tmp_, tmp_, var_, ALU.mult)
                v.drain()
                nc.vector.tensor_scalar(tmp_, tmp_, -0.5, 1.5, ALU.mult, ALU.add)
                v.drain()
                nc.vector.tensor_tensor(rstd_, rstd_, tmp_, ALU.mult)
            v.drain()

        def stats(v, tiles):
            for t, x_ in enumerate(tiles):
                nc.vector.bn_stats(st[:, 6 * t:6 * t + 6], x_)
            v.drain()
            n = len(tiles)
            moments(v, st[:, 0:6 * n], mean[:, 0:n], rstd[:, 0:n], var[:, 0:n], nt1[:, 0:n])

        def normalise(out, x_, t):
            return nc.vector.tensor_scalar(out, x_, mean[:, t:t + 1], rstd[:, t:t + 1], ALU.subtract, ALU.mult)

        def load_tile_sched(eng, d):
            cs = eng.value_load(sched[0:1, ds(d, 1)], min_val=0, max_val=NCH)
            ce = eng.value_load(sched[0:1, ds(P + d, 1)], min_val=0, max_val=NCH)
            off = eng.value_load(sched[0:1, ds(2 * P + d, 1)], min_val=0, max_val=NT * NCH)
            return cs, ce, off

        def xt(d):
            return xs[:, ds(d * D, D)]

        def gather(p, L):
            passes = p.value_load(sched[0:1, 3 * P:3 * P + 1], min_val=1, max_val=NT)
            with p.Fori(0, passes) as turn:
                with p.Fori(0, T // RT) as it:
                    m = p.snap(turn * (T // RT) + it)
                    for half in range(2):
                        p.wait_ge(L.landed, m * RT + half * RC)
                        nc.gpsimd.tensor_copy(idxs[:, half * RC:half * RC + RC],
                                              srcs[:, ds(it * RT + half * RC, RC)]).then_inc(L.idx_set, 1)
                        p.wait_ge(L.idx_set, m * 2 + half + 1)
                        for k in range(half * RC, half * RC + RC):
                            if k % 2 == 0:
                                hold(p, L.ring_free, m * RC + k // 2)
                            nc.gpsimd.indirect_dma_start(
                                out=ring[:, k * RW:k * RW + D], out_offset=None, in_=L.rows,
                                in_offset=bass.IndirectOffsetOnAxis(ap=idxs[:, k:k + 1], axis=0),
                            ).then_inc(L.slot[k], 16)

        def relay(s, L):
            passes = s.value_load(sched[0:1, 3 * P:3 * P + 1], min_val=1, max_val=NT)
            s.sem_inc(L.landed, RC)
            with s.Fori(0, passes) as turn:
                with s.Fori(0, T // RT) as it:
                    m = s.snap(turn * (T // RT) + it)
                    for k in range(RT):
                        s.wait_ge(L.slot[k], m * 16 + 16)
                        s.sem_inc(L.landed, 1)

        def onehots(v, L, layer, d):
            cs, ce, off = load_tile_sched(v, d)
            v.drain()
            nc.vector.tensor_scalar(iota[:], iota[:], float(P), None, ALU.add)
            v.drain()

            def pair(first, q):
                for j in range(2):
                    v.wait_ge(L.used[j], q)
                    col = dsts[:, ds(first + j, 1)]
                    if layer == 0:
                        nc.vector.tensor_scalar(S[j][:], iota[:], col, wts_col(first + j),
                                                ALU.is_equal, ALU.mult).then_inc(L.made[j], 1)
                    else:
                        nc.vector.tensor_scalar(S[j][:], iota[:], col, None, ALU.is_equal).then_inc(L.made[j], 1)

            def wts_col(c):
                return wts[:, ds(c - 2, 1)]

            q0 = v.snap(cs + off + d)
            for j in range(2):
                v.wait_ge(L.used[j], q0)
                col = dsts[:, ds(cs * 2 + j, 1)]
                if layer == 0:
                    prev = v.snap((cs * 2 + (T - 2)) % T, min_val=0, max_val=T - 2)
                    nc.vector.tensor_scalar(S[j][:], iota[:], col, wts[:, ds(prev + j, 1)],
                                            ALU.is_equal, ALU.mult).then_inc(L.made[j], 1)
                else:
                    nc.vector.tensor_scalar(S[j][:], iota[:], col, None, ALU.is_equal).then_inc(L.made[j], 1)
            with v.If(cs < ce):
                with v.Fori(cs, ce) as c:
                    g = v.snap(c + off)
                    q = v.snap(g + d + 1)
                    if layer == 1:
                        v.wait_ge(L.landed, g * 2 + 2 + RC)
                        slot = v.snap((g & (RC - 1)) * (2 * RW), min_val=0, max_val=(RC - 1) * 2 * RW)
                        for j in range(2):
                            nc.vector.tensor_scalar(ring[:, ds(slot + (j * RW + D), NREL)], rel_iota[:],
                                                    rels[:, ds(c * 2 + j, 1)], None, ALU.is_equal)
                    for j in range(2):
                        v.wait_ge(L.used[j], q)
                        if j == 1:
                            v.sem_inc(L.ring_free, 1)
                        col = dsts[:, ds(c * 2 + (2 + j), 1)]
                        if layer == 0:
                            nc.vector.tensor_scalar(S[j][:], iota[:], col, wts[:, ds(c * 2 + j, 1)],
                                                    ALU.is_equal, ALU.mult).then_inc(L.made[j], 1)
                        else:
                            nc.vector.tensor_scalar(S[j][:], iota[:], col, None,
                                                    ALU.is_equal).then_inc(L.made[j], 1)
            return v.snap(ce + off + d + 1)

        def segment_sum(pe, L, d, out, width):
            cs, ce, off = load_tile_sched(pe, d)
            g0 = pe.snap(cs + off)
            q0 = pe.snap(g0 + d + 1)
            before = pe.snap(((g0 + (RC - 1)) & (RC - 1)) * (2 * RW), min_val=0, max_val=(RC - 1) * 2 * RW)
            for j in range(2):
                pe.wait_ge(L.made[j], q0)
                nc.tensor.matmul(out[:, 0:width], S[j][:], ring[:, ds(before + j * RW, width)],
                                 start=(j == 0), stop=True, skip_group_check=True).then_inc(L.used[j], 1)
            with pe.If(cs < ce):
                with pe.Fori(cs, ce) as c:
                    g = pe.snap(c + off)
                    pe.wait_ge(L.landed, g * 2 + 2 + RC)
                    slot = pe.snap((g & (RC - 1)) * (2 * RW), min_val=0, max_val=(RC - 1) * 2 * RW)
                    for j in range(2):
                        pe.wait_ge(L.made[j], g + d + 2)
                        nc.tensor.matmul(out[:, 0:width], S[j][:], ring[:, ds(slot + j * RW, width)],
                                         start=False, stop=True, skip_group_check=True).then_inc(L.used[j], 1)

        def mm(out, lhsT, rhs, start, stop):
            return nc.tensor.matmul(out, lhsT, rhs, start=start, stop=stop, skip_group_check=True)

        def transposes(out, tiles):
            w = P * len(tiles)
            for t, x_ in enumerate(tiles):
                for k in range(KD):
                    last = nc.tensor.transpose(out[:, k * w + t * P:k * w + t * P + P], x_[:, k * P:k * P + P], ident[:])
            return last

        with nc.Block() as block:

            @block.sync
            def _(s):
                s.dma_start(srcs[:], a["src_tiles"]).then_inc(tables_in, 16)
                s.dma_start(dsts[:, 2:2 + T].bitcast(i32), a["dst_tiles"]).then_inc(tables_in, 16)
                s.dma_start(wts[:], a["w_tiles"]).then_inc(tables_in, 16)
                s.dma_start(rels[:].bitcast(i32), a["rel_tiles"]).then_inc(tables_in, 16)
                s.dma_start(ring[:, 0:T].bitcast(i32), a["dst_flat"]).then_inc(tables_in, 16)
                s.dma_start(ring[:, T:T + 1].bitcast(i32), a["dst_next"]).then_inc(tables_in, 16)
                s.dma_start(small[0:FP, 0:FK].bitcast(i32), a["dst_firsts"]).then_inc(tables_in, 16)
                for dst_, src_ in ((wg, "wg"), (gbias[:], None), (w1_0, "w1_0"), (w2_0, "w2_0"), (rwT[:], "rwT"),
                                   (b1_0[:], "b1_0"), (b2_0[:], "b2_0"), (gateT[:], "gateT"), (gateb[:], "gateb"),
                                   (bih[:], "b_ih"), (bhh[:], "b_hh")):
                    src_ = a["gbias"].partition_broadcast(P) if src_ is None else a[src_]
                    s.dma_start(dst_, src_).then_inc(weights0_in, 16)
                s.wait_ge(x_cleared, 1)
                xr = a["x"][0:(NT - 1) * P, :].rearrange("(n p) f -> p n f", p=P)
                for c in range(XCH):
                    n0, n1 = c * XT, min((c + 1) * XT, NT - 1)
                    s.dma_start(xs[:, n0 * D:n1 * D].rearrange("p (n f) -> p n f", f=D), xr[:, n0:n1, :]).then_inc(x_in[c], 16)
                s.dma_start(xs[0:LAST, (NT - 1) * D:NT * D], a["x"][(NT - 1) * P:N, :]).then_inc(x_in[XCH], 16)
                for c in range(XCH):
                    s.wait_ge(x_in[c], 16)
                    if c == XCH - 1:
                        s.wait_ge(x_in[XCH], 16)
                    s.sem_inc(x_chunks, 1)
                with s.Fori(0, NPAIR) as i:
                    s.wait_ge(p_out, i + 1)
                    s.dma_start(hw_t[:, ds(i * 2, 2), :], pairo[:].rearrange("p (t f) -> p t f", t=2)).then_inc(p_st, 16)
                s.wait_ge(p_st, 16 * NPAIR)
                s.sem_inc(hw_stored, 1)
                s.wait_ge(sched_made, 1)
                relay(s, L0)
                s.wait_ge(mm2_done, 9 * NPAIR)
                s.wait_ge(tT_ready, NPAIR)
                s.wait_ge(acc_done, 9 * NPAIR)
                s.wait_ge(gelu_done, 8 * NPAIR)
                s.dma_start(wih, a["w_ihT"]).then_inc(weights1_in, 16)
                s.dma_start(whh, a["w_hhT"]).then_inc(weights1_in, 16)
                s.dma_start(relT, a["relT"]).then_inc(weights1_in, 16)
                relay(s, L1)
                s.wait_ge(x3_stored, 1)
                s.dma_start(be1, a["b1_1"]).then_inc(be1_in, 16)
                with s.Fori(0, NE1 // 2) as ep:
                    for b in range(2):
                        s.wait_ge(e_used, ep * 2 + b)
                        e = ep * 2 + b
                        s.dma_start(we1[b], a["w1_1"][ds(e, 1), :, :].rearrange("o p f -> (o p) f")).then_inc(we_in[b], 16)
                        s.dma_start(we2[b], a["w2_1"][ds(e, 1), :, :].rearrange("o p f -> (o p) f")).then_inc(we_in[b], 16)
                        s.dma_start(be2[b], a["b2_1"][ds(e, 1), :].to_broadcast((P, D))).then_inc(we_in[b], 16)
                for b in range(2):
                    for t in range(4):
                        s.wait_ge(scat[b][t], 16 * (NE1 * GROUPS // 2))

            @block.gpsimd
            def _(p):
                nc.gpsimd.memset(xs[:, (NT - 1) * D:NT * D], 0.0).then_inc(x_cleared, 1)
                nc.gpsimd.memset(ident[:], 0.0).then_inc(consts_made, 1)
                nc.gpsimd.memset(ones[:], 1.0).then_inc(consts_made, 1)
                nc.gpsimd.memset(upper[:], 1.0).then_inc(consts_made, 1)
                nc.gpsimd.iota(iota0[:], pattern=[[1, P]], base=0, channel_multiplier=0,
                               allow_small_or_imprecise_dtypes=True).then_inc(consts_made, 1)
                nc.gpsimd.iota(iota[:], pattern=[[1, P]], base=-P, channel_multiplier=0,
                               allow_small_or_imprecise_dtypes=True).then_inc(consts_made, 1)
                nc.gpsimd.iota(rel_iota[:], pattern=[[1, NREL]], base=0, channel_multiplier=0,
                               allow_small_or_imprecise_dtypes=True).then_inc(consts_made, 1)
                nc.gpsimd.iota(tok1[:], pattern=[[P, 2]], base=1 - 2 * P, channel_multiplier=1,
                               allow_small_or_imprecise_dtypes=True).then_inc(consts_made, 1)
                nc.gpsimd.memset(dsts[:, 0:2], float(FAR)).then_inc(consts_made, 1)
                nc.gpsimd.memset(e16[:], 0.0).then_inc(consts_made, 1)
                nc.gpsimd.memset(invt[:], 0.0).then_inc(consts_made, 1)
                nc.gpsimd.memset(ohs[:], 0.0).then_inc(consts_made, 1)
                nc.gpsimd.iota(small[:, 128:128 + NT], pattern=[[P, NT]], base=P, channel_multiplier=0,
                               allow_small_or_imprecise_dtypes=True).then_inc(consts_made, 1)
                p.wait_ge(consts_made, 12)
                nc.gpsimd.affine_select(out=ident[:], in_=ident[:], compare_op=ALU.not_equal, fill=1.0, base=0,
                                        pattern=[[-1, P]], channel_multiplier=1).then_inc(consts_made, 1)
                nc.gpsimd.affine_select(out=upper[:], in_=upper[:], compare_op=ALU.is_ge, fill=0.0, base=0,
                                        pattern=[[1, P]], channel_multiplier=-1).then_inc(consts_made, 1)
                nc.gpsimd.memset(e16[:, 16:17], 1.0).then_inc(consts_made, 1)
                p.wait_ge(weights0_in, 16 * 11)
                with p.Fori(0, NPAIR) as i:
                    p.wait_ge(p_tn, i + 1)
                    for t in range(2):
                        last = nc.gpsimd.tensor_tensor(xt(i * 2 + t), xt(i * 2 + t), gbias[:], ALU.add)
                    last.then_inc(x_biased, 1)
                p.wait_ge(sched_made, 1)
                nc.gpsimd.memset(ring[:], 0.0).then_inc(ring_clear, 1)
                p.wait_ge(ring_clear, 1)
                p.wait_ge(hw_stored, 1)
                gather(p, L0)
                p.wait_ge(h1_stored, 1)
                p.wait_ge(L0.agg_free, NPAIR)
                gather(p, L1)
                p.wait_ge(e_consts, 1)

                def fetch(grp, b):
                    nc.gpsimd.tensor_copy(gidx[:, 4 * b:4 * b + 4], tokg[:, ds(grp * 4, 4)]).then_inc(e_idx, 1)
                    hold(p, e_idx, grp + 1)
                    for t in range(4):
                        nc.gpsimd.indirect_dma_start(
                            out=xg[b][:, t * D:t * D + D], out_offset=None, in_=x3_d,
                            in_offset=bass.IndirectOffsetOnAxis(ap=gidx[:, 4 * b + t:4 * b + t + 1], axis=0),
                        ).then_inc(xg_in[b][t], 16)

                def put(grp, b):
                    p.wait_ge(e_out, grp + 1)
                    nc.gpsimd.tensor_copy(sidx[:, 4 * b:4 * b + 4], toks[:, ds(grp * 4, 4)]).then_inc(e_issued, 1)
                    hold(p, e_issued, grp + 1)
                    for t in range(4):
                        nc.gpsimd.indirect_dma_start(
                            out=a["out"], out_offset=bass.IndirectOffsetOnAxis(ap=sidx[:, 4 * b + t:4 * b + t + 1], axis=0),
                            in_=yo[b][:, t * D:t * D + D], in_offset=None, bounds_check=N - 1, oob_is_err=False,
                        ).then_inc(scat[b][t], 16)

                NG = NE1 * GROUPS
                fetch(0, 0)
                fetch(1, 1)
                with p.Fori(0, NG // 2 - 1) as h:
                    for b in range(2):
                        put(h * 2 + b, b)
                        for t in range(4):
                            p.wait_ge(scat[b][t], h * 16 + 16)
                        fetch(h * 2 + b + 2, b)
                for b in range(2):
                    put(NG - 2 + b, b)
                    for t in range(4):
                        p.wait_ge(scat[b][t], 16 * (NG // 2))

            @block.vector
            def _(v):
                v.wait_ge(consts_made, 15)
                v.wait_ge(tables_in, 16 * 7)
                nc.vector.tensor_copy(dsts[:, 2:2 + T], dsts[:, 2:2 + T].bitcast(i32))
                nc.vector.tensor_copy(rels[:], rels[:].bitcast(i32))
                nc.vector.tensor_copy(small[0:FP, 8:8 + FK], small[0:FP, 0:FK].bitcast(i32))
                fall = ring[:, T + 8:2 * T + 8]
                nc.vector.tensor_tensor(fall, ring[:, 0:T].bitcast(i32), ring[:, 1:T + 1].bitcast(i32), ALU.is_gt)
                v.drain()
                nc.vector.reduce_max(small[:, 16:17], fall, AX.X)
                cnt = small[0:FP, 128:128 + NT]
                acc = ring[0:FP, 0:NT]
                nc.vector.tensor_scalar(acc, cnt, small[0:FP, 8:9], None, ALU.is_gt)
                for k in range(1, FK):
                    v.drain()
                    nc.vector.scalar_tensor_tensor(out=acc, in0=cnt, scalar=small[0:FP, 8 + k:9 + k], in1=acc,
                                                   op0=ALU.is_gt, op1=ALU.add)
                v.drain()
                nc.vector.tensor_copy(small[0:FP, 16 + 1:16 + 2], small[0:FP, 16:17]).then_inc(cnt_made, 1)
                v.wait_ge(cnt_read, 1)
                row = small[0:1, :]
                nc.vector.tensor_copy(row[:, 0:NT], bank[0][0:1, 0:NT])
                nc.vector.tensor_scalar(row[:, 127:128], bank[0][0:1, 256:257], 1.0, None, ALU.min)
                v.drain()
                nc.vector.memset(row[:, NT - 1:NT], float(NCH))
                nc.vector.tensor_scalar(row[:, 126:127], row[:, 127:128], -1.0, 1.0, ALU.mult, ALU.add)
                nc.vector.tensor_scalar(row[:, 125:126], row[:, 127:128], float(NCH), None, ALU.mult)
                nc.vector.tensor_scalar(row[:, 124:125], row[:, 127:128], float(NT - 1), 1.0, ALU.mult, ALU.add)
                nc.vector.tensor_scalar(row[:, 123:124], row[:, 127:128], float(NCH) / P, None, ALU.mult)
                v.drain()
                nc.vector.memset(sched[:], 0)
                v.drain()
                nc.vector.tensor_scalar(sched[:, 1:NT], row[:, 0:NT - 1], row[:, 126:127], None, ALU.mult)
                nc.vector.tensor_scalar(sched[:, P:P + NT], row[:, 0:NT], row[:, 126:127], row[:, 125:126],
                                        ALU.mult, ALU.add)
                nc.vector.tensor_scalar(sched[:, 2 * P:2 * P + NT], iota0[0:1, 0:NT], row[:, 125:126], None, ALU.mult)
                nc.vector.tensor_copy(sched[:, 3 * P:3 * P + 1], row[:, 124:125])
                v.drain()
                nc.vector.tensor_copy(small[:, 0:1], ones[:, 0:1]).then_inc(sched_made, 1)
                stx, meanx = ring[:, 0:6 * NT], ring[:, 6 * NT:7 * NT]
                varx, rx, tmpx = ring[:, 8 * NT:9 * NT], ring[:, 9 * NT:10 * NT], ring[:, 10 * NT:11 * NT]
                with v.Fori(0, XCH) as c:
                    hold(v, x_chunks, c + 1)
                    with v.Fori(0, XT) as d:
                        nc.vector.bn_stats(stx[:, ds((c * XT + d) * 6, 6)], xt(c * XT + d))
                v.drain()
                moments(v, stx, meanx, rx, varx, tmpx)
                with v.Fori(0, NPAIR) as i:
                    v.wait_ge(p_tr, i)
                    for t in range(2):
                        d = i * 2 + t
                        last = nc.vector.tensor_scalar(tn[:, t * D:t * D + D], xt(d), meanx[:, ds(d, 1)],
                                                       rx[:, ds(d, 1)], ALU.subtract, ALU.mult)
                    last.then_inc(p_tn, 1)
                v.drain()
                nc.vector.tensor_copy(small[:, 0:1], ones[:, 0:1]).then_inc(sched_made, 1)

                def start_layer(L):
                    v.sem_inc(L.ring_free, RC - 3)

                def epilogue0(i, q):
                    v.wait_ge(L0.used[1], q)
                    if isinstance(i, int) and i == 0:
                        v.wait_ge(x_biased, NPAIR)
                    for t in range(2):
                        last = nc.vector.tensor_tensor(xt(i * 2 + t), agg[t][:, 0:D], xt(i * 2 + t), ALU.add)
                    last.then_inc(L0.agg_free, 1)
                    v.drain()
                    stats(v, [xt(i * 2), xt(i * 2 + 1)])
                    v.wait_ge(t_tr, i)
                    for t in range(2):
                        last = normalise(tn[:, t * D:t * D + D], xt(i * 2 + t), t)
                    last.then_inc(t_ready, 1)
                    v.drain()
                    for t in range(2):
                        nc.vector.tensor_tensor(xt(i * 2 + t), xt(i * 2 + t), tn[:, t * D:t * D + D], ALU.add)
                    v.drain()

                lg, ex, pr, m8, comb = (small[:, 16 * k:16 * k + 16] for k in range(5))
                rs = small[:, 80:96]

                def softmax_shift(logits, ready, shifted, i, src_bank):
                    hold(v, ready, i + 1)
                    for t in range(2):
                        nc.vector.max(m8[:, 8 * t:8 * t + 8], src_bank[:, 8 * t:8 * t + 8])
                    v.drain()
                    for t in range(2):
                        last = nc.vector.tensor_scalar(lg[:, 8 * t:8 * t + 8], src_bank[:, 8 * t:8 * t + 8],
                                                       m8[:, 8 * t:8 * t + 1], None, ALU.subtract)
                    last.then_inc(shifted, 1)

                def softmax_rest(done, i):
                    v.wait_ge(done, i + 1)
                    nc.vector.reduce_sum(rs[:, 0:2], ex.rearrange("p (t e) -> p t e", t=2), AX.X)
                    v.drain()
                    nc.vector.reciprocal(rs[:, 2:4], rs[:, 0:2])
                    v.drain()
                    for t in range(2):
                        nc.vector.tensor_scalar(pr[:, 8 * t:8 * t + 8], ex[:, 8 * t:8 * t + 8],
                                                rs[:, 2 + t:3 + t], None, ALU.mult)
                    v.drain()
                    for t in range(2):
                        nc.vector.max(m8[:, 8 * t:8 * t + 8], pr[:, 8 * t:8 * t + 8])
                    v.drain()
                    for t in range(2):
                        nc.vector.max_index(smalli[:, 8 * t:8 * t + 8], m8[:, 8 * t:8 * t + 8], pr[:, 8 * t:8 * t + 8])
                    v.drain()
                    nc.vector.tensor_copy(small[:, 96:112], smalli[:, 0:16])
                    v.drain()

                def combine(j):
                    softmax_shift(lg, lg_ready, ls_ready, j, bank[7])
                    softmax_rest(ex_ready, j)
                    for t in range(2):
                        nc.vector.tensor_tensor(rs[:, 4 + t:5 + t], m8[:, 8 * t:8 * t + 1], m8[:, 8 * t + 1:8 * t + 2], ALU.add)
                    v.drain()
                    nc.vector.tensor_scalar(rs[:, 4:6], rs[:, 4:6], 1e-12, None, ALU.max)
                    v.drain()
                    nc.vector.reciprocal(rs[:, 6:8], rs[:, 4:6])
                    v.drain()
                    for t in range(2):
                        nc.vector.tensor_scalar(rs[:, 8 + 2 * t:10 + 2 * t], m8[:, 8 * t:8 * t + 2],
                                                rs[:, 6 + t:7 + t], None, ALU.mult)
                    v.drain()
                    for t in range(2):
                        nc.vector.tensor_scalar(comb[:, 8 * t:8 * t + 8], iota0[:, 0:8], small[:, 96 + 8 * t:97 + 8 * t],
                                                rs[:, 8 + 2 * t:9 + 2 * t], ALU.is_equal, ALU.mult)
                        nc.vector.tensor_scalar(pr[:, 8 * t:8 * t + 8], iota0[:, 0:8], small[:, 97 + 8 * t:98 + 8 * t],
                                                rs[:, 9 + 2 * t:10 + 2 * t], ALU.is_equal, ALU.mult)
                    v.drain()
                    nc.vector.tensor_tensor(comb, comb, pr, ALU.add).then_inc(comb_ready, 1)
                    v.drain()

                def accumulate(j, item):
                    y = bank[5 + item % 2]
                    v.wait_ge(mm2_done, j * 9 + item + 1)
                    for t in range(2):
                        x_ = xt(j * 2 + t)
                        if item < 8:
                            last = nc.vector.scalar_tensor_tensor(
                                out=x_, in0=y[:, t * D:t * D + D], scalar=comb[:, 8 * t + item:8 * t + item + 1],
                                in1=x_, op0=ALU.mult, op1=ALU.add)
                        else:
                            last = nc.vector.tensor_tensor(x_, y[:, t * D:t * D + D], x_, ALU.add)
                    last.then_inc(acc_done, 1)
                    v.drain()

                def normalise_h1(k):
                    stats(v, [xt(k * 2), xt(k * 2 + 1)])
                    v.wait_ge(h1_store, k * 16)
                    for t in range(2):
                        last = normalise(pairo[:, t * D:t * D + D], xt(k * 2 + t), t)
                    last.then_inc(h1_ready, 1)

                def layer0(i, inner, ffn, norm):
                    if inner:
                        onehots(v, L0, 0, i * 2)
                        q = onehots(v, L0, 0, i * 2 + 1)
                    if ffn:
                        combine(i - 1)
                    if inner:
                        epilogue0(i, q)
                    if ffn:
                        accumulate(i - 1, 0)
                        accumulate(i - 1, 1)
                    if norm:
                        normalise_h1(i - 2)
                    if ffn:
                        for item in range(2, 9):
                            accumulate(i - 1, item)

                v.wait_ge(hw_stored, 1)
                start_layer(L0)
                layer0(0, True, False, False)
                layer0(1, True, True, False)
                with v.Fori(2, NPAIR) as i:
                    layer0(i, True, True, True)
                layer0(NPAIR, False, True, True)
                layer0(NPAIR + 1, False, False, True)

                v.drain()
                nc.vector.tensor_scalar(iota[:], iota0[:], -float(P), None, ALU.add)
                for t in range(2):
                    nc.vector.memset(red[t][:, 272:273], 1.0)
                v.drain()
                nc.vector.tensor_copy(small[:, 0:1], ones[:, 0:1]).then_inc(l1_consts, 1)
                start_layer(L1)

                def gru_pre(j, t):
                    nb = bank[3 + 2 * t]
                    v.wait_ge(g_tanh, j * 2 + t + 1)
                    nc.vector.scalar_tensor_tensor(out=ga[t], in0=gates[t][:, 0:D], scalar=1.0, in1=nb[:, D:2 * D],
                                                   op0=ALU.add, op1=ALU.mult)
                    v.drain()
                    nc.vector.scalar_tensor_tensor(out=ga[t], in0=ga[t], scalar=0.5, in1=nb[:, 0:D],
                                                   op0=ALU.mult, op1=ALU.add).then_inc(g_pre, 1)

                def gru_post(j):
                    v.wait_ge(g_n, j * 2 + 2)
                    for t in range(2):
                        nc.vector.tensor_tensor(ga[t], hin[:, t * D:t * D + D], gn[t], ALU.subtract)
                        nc.vector.tensor_tensor(xt(j * 2 + t), xt(j * 2 + t), gn[t], ALU.add)
                    v.drain()
                    for t in range(2):
                        nc.vector.scalar_tensor_tensor(out=ga[t], in0=gates[t][:, D:2 * D], scalar=1.0, in1=ga[t],
                                                       op0=ALU.add, op1=ALU.mult)
                    v.drain()
                    for t in range(2):
                        last = nc.vector.scalar_tensor_tensor(out=xt(j * 2 + t), in0=ga[t], scalar=0.5, in1=xt(j * 2 + t),
                                                              op0=ALU.mult, op1=ALU.add)
                    last.then_inc(x3_ready, 1)
                    v.drain()
                    stats(v, [xt(j * 2), xt(j * 2 + 1)])
                    v.wait_ge(r_tr, j)
                    for t in range(2):
                        last = normalise(tn[:, t * D:t * D + D], xt(j * 2 + t), t)
                    last.then_inc(r_t, 1)

                def route_expert(k):
                    softmax_shift(lg, r_lg, r_ls, k, bank[7])
                    softmax_rest(r_ex, k)
                    for t in range(2):
                        last = nc.vector.tensor_scalar(ohs[:, 8 * t:8 * t + 8], iota0[:, 0:8],
                                                       small[:, 96 + 8 * t:97 + 8 * t], None, ALU.is_equal)
                    last.then_inc(r_oh, 1)

                pos, posi = small[:, 112:128], smalli[:, 16:32].bitcast(i32)

                def route_slot(k):
                    v.wait_ge(r_pos, k + 1)
                    nc.vector.tensor_tensor(comb, ohs[:, 0:16], bank[7][:, 16:32], ALU.mult)
                    nc.vector.tensor_tensor(ohs[:, 16:24], ohs[:, 16:24], ohs[:, 0:8], ALU.add)
                    nc.vector.tensor_scalar(tok1[:], tok1[:], 2.0 * P, None, ALU.add)
                    v.drain()
                    nc.vector.tensor_tensor(ohs[:, 16:24], ohs[:, 16:24], ohs[:, 8:16], ALU.add)
                    nc.vector.reduce_sum(pos[:, 0:2], comb.rearrange("p (t e) -> p t e", t=2), AX.X)
                    v.drain()
                    nc.vector.tensor_scalar(posi[:, 0:2], pos[:, 0:2], -1.0, None, ALU.add)
                    nc.vector.tensor_scalar(pos[:, 2:4], pos[:, 0:2], float(CAP), 1024.0, ALU.is_gt, ALU.mult)
                    v.drain()
                    nc.vector.tensor_scalar(posi[:, 2:4], posi[:, 0:2], 7, None, ALU.logical_shift_right)
                    nc.vector.tensor_scalar(posi[:, 4:6], posi[:, 0:2], 127, None, ALU.bitwise_and)
                    v.drain()
                    nc.vector.tensor_copy(pos[:, 4:6], posi[:, 4:6])
                    nc.vector.tensor_copy(pos[:, 6:8], posi[:, 2:4])
                    v.drain()
                    nc.vector.tensor_tensor(pos[:, 6:8], pos[:, 6:8], pos[:, 2:4], ALU.add)
                    v.drain()
                    for t in range(2):
                        nc.vector.tensor_scalar(pos[:, 8 + t:9 + t], small[:, 96 + 8 * t:97 + 8 * t],
                                                float(4 * GROUPS), pos[:, 6 + t:7 + t], ALU.mult, ALU.add)
                    v.drain()
                    for t in range(2):
                        nc.vector.tensor_scalar(ohlo[t], iota0[:], pos[:, 4 + t:5 + t], None, ALU.is_equal)
                        nc.vector.tensor_scalar(ohhi[t][:, 0:P], iota0[:], pos[:, 8 + t:9 + t], tok1[:, t:t + 1],
                                                ALU.is_equal, ALU.mult)
                        last = nc.vector.tensor_scalar(ohhi[t][:, P:2 * P], iota0[:], pos[:, 8 + t:9 + t],
                                                       m8[:, 8 * t:8 * t + 1], ALU.is_equal, ALU.mult)
                    last.then_inc(r_slot, 1)

                def route_add(k):
                    v.wait_ge(r_inv, k + 1)
                    nc.vector.tensor_tensor(invt[:], invt[:], bank[7][:, 256:512], ALU.add).then_inc(r_done, 1)

                def layer1(i, inner, gru, route):
                    if inner:
                        onehots(v, L1, 1, i * 2)
                        q = onehots(v, L1, 1, i * 2 + 1)
                        v.wait_ge(L1.used[1], q)
                        v.sem_inc(L1.agg_ready, 1)
                    if route:
                        route_expert(i - 2)
                    if gru:
                        gru_pre(i - 1, 0)
                    if route:
                        route_slot(i - 2)
                    if gru:
                        gru_pre(i - 1, 1)
                        gru_post(i - 1)
                    if route:
                        route_add(i - 2)

                layer1(0, True, False, False)
                layer1(1, True, True, False)
                with v.Fori(2, NPAIR) as i:
                    layer1(i, True, True, True)
                layer1(NPAIR, False, True, True)
                layer1(NPAIR + 1, False, False, True)

                v.wait_ge(x3_stored, 1)
                v.drain()
                nc.vector.tensor_scalar(tokg, invt[:, 0:P], -1.0, 0.0, ALU.add, ALU.max)
                nc.vector.tensor_scalar(yo[0][:, 0:P], invt[:, 0:P], 0.0, float(FAR), ALU.is_equal, ALU.mult)
                nc.vector.tensor_scalar(yo[1][:, 0:P], invt[:, 0:P], -1.0, None, ALU.add)
                nc.vector.memset(c1e4, 1e4)
                nc.vector.memset(cm1e4, -1e4)
                v.drain()
                nc.vector.tensor_tensor(toks, yo[0][:, 0:P], yo[1][:, 0:P], ALU.add)
                v.drain()
                nc.vector.tensor_copy(small[:, 0:1], ones[:, 0:1]).then_inc(e_consts, 1)

                def norm_group(grp, b, h):
                    for t in range(4):
                        v.wait_ge(xg_in[b][t], h * 16 + 16)
                    stats(v, [xg[b][:, t * D:t * D + D] for t in range(4)])
                    v.wait_ge(e_tr, grp)
                    for t in range(4):
                        last = normalise(xn[:, t * D:t * D + D], xg[b][:, t * D:t * D + D], t)
                    last.then_inc(e_norm, 1)

                def finish_group(grp, b, be):
                    for t in range(4):
                        v.wait_ge(e_y, grp * 4 + t // 2 * 2 + 2)
                        y = bank[5 + t // 2][:, (t % 2) * D:(t % 2) * D + D]
                        nc.vector.tensor_tensor(ya, y, be, ALU.add)
                        nc.vector.memset(yz, 0.0)
                        v.drain()
                        nc.vector.tensor_scalar(ya, ya, invt[:, ds(grp * 4 + (P + t), 1)], None, ALU.mult)
                        v.drain()
                        nc.vector.tensor_tensor(ym, ya, ya, ALU.is_equal)
                        v.drain()
                        nc.vector.copy_predicated(yz, ym, ya)
                        v.drain()
                        nc.vector.tensor_scalar(ym, yz, BIG, None, ALU.is_gt)
                        v.drain()
                        nc.vector.copy_predicated(yz, ym, c1e4)
                        v.drain()
                        nc.vector.tensor_scalar(ym, yz, -BIG, None, ALU.is_lt)
                        v.drain()
                        nc.vector.copy_predicated(yz, ym, cm1e4)
                        v.drain()
                        last = nc.vector.tensor_tensor(yo[b][:, t * D:t * D + D], yz, xg[b][:, t * D:t * D + D], ALU.add)
                        if t == 3:
                            last.then_inc(e_out, 1)
                        v.drain()

                norm_group(0, 0, 0)
                with v.Fori(0, NE1 // 2) as ep:
                    for be in range(2):
                        v.wait_ge(we_in[be], ep * 48 + 48)
                        for g in range(GROUPS):
                            grp = (ep * 2 + be) * GROUPS + g
                            h = ep * GROUPS + (be * GROUPS + g) // 2
                            b = g % 2
                            if be == 1 and g == GROUPS - 1:
                                with v.If(ep < NE1 // 2 - 1):
                                    norm_group(grp + 1, 1 - b, h + 1)
                            else:
                                norm_group(grp + 1, 1 - b, h + b)
                            finish_group(grp, b, be2[be])

            @block.scalar
            def _(act):
                def copy(out, in_):
                    return nc.scalar.activation(out, in_, ACT.Copy)

                with act.Fori(0, NPAIR) as i:
                    act.wait_ge(p_tr, i + 1)
                    act.wait_ge(p_mm, i)
                    copy(tT[:], bank[2][:]).then_inc(p_tT, 1)
                    act.wait_ge(p_mm, i + 1)
                    act.wait_ge(p_st, i * 16)
                    copy(pairo[:], bank[3][:]).then_inc(p_out, 1)

                ex, lg = small[:, 16:32], small[:, 0:16]

                def exps(shifted, done, j):
                    act.wait_ge(shifted, j + 1)
                    nc.scalar.activation(ex, lg, ACT.Exp).then_inc(done, 1)

                def layer0(i, inner, ffn, norm):
                    if ffn:
                        j = i - 1
                        exps(ls_ready, ex_ready, j)
                        for e in range(NE0):
                            act.wait_ge(h_ready, j * 8 + e + 1)
                            act.wait_ge(mm2_done, j * 9 + max(e - 1, 0))
                            for c in range(2):
                                last = nc.scalar.activation(hT[e % 2][:, c * D:c * D + D],
                                                            bank[3 + e % 2][:, c * D:c * D + D], ACT.Gelu,
                                                            bias=b1_0[:, 2 * e + c:2 * e + c + 1])
                            last.then_inc(gelu_done, 1)
                        act.wait_ge(combT_tr, j + 1)
                        copy(combT[:], bank[7][0:NE0, 128:128 + 2 * P]).then_inc(combT_in, 1)
                    if inner:
                        act.wait_ge(t_tr, i + 1)
                        copy(tT[:], bank[2][:]).then_inc(tT_ready, 1)
                    if norm:
                        k = i - 2
                        act.wait_ge(h1_ready, k + 1)
                        act.dma_start(h1_t[:, ds(k * 2, 2), :], pairo[:].rearrange("p (t f) -> p t f", t=2)).then_inc(h1_store, 16)

                act.wait_ge(weights0_in, 16 * 11)
                layer0(0, True, False, False)
                layer0(1, True, True, False)
                with act.Fori(2, NPAIR) as i:
                    layer0(i, True, True, True)
                layer0(NPAIR, False, True, True)
                layer0(NPAIR + 1, False, False, True)
                act.wait_ge(h1_store, 16 * NPAIR)
                act.sem_inc(h1_stored, 1)

                act.wait_ge(relw_mm, 1)
                act.wait_ge(l1_consts, 1)
                for g in range(2):
                    last = copy(relw[:, 512 * g:512 * g + 512], bank[3 + g][0:17, :])
                last.then_inc(relw_in, 1)

                def layer1(i, inner, gru, route):
                    if gru:
                        j = i - 1
                        act.dma_start(hin.rearrange("p (t f) -> p t f", t=2), h1_t[:, ds(j * 2, 2), :]).then_inc(hin_in, 16)
                        act.wait_ge(L1.agg_ready, j + 1)
                        for t in range(2):
                            copy(red[t][:, 0:272], agg[t][:, 0:272]).then_inc(red_in, 1)
                    if route:
                        k = i - 2
                        act.wait_ge(r_tr, k + 1)
                        copy(tT[:], bank[2][:]).then_inc(r_T, 1)
                        exps(r_ls, r_ex, k)
                    if gru:
                        for t in range(2):
                            act.wait_ge(g_tr, j * 2 + t + 1)
                            copy(cT[t], agg[t][0:17, 384:512])
                            copy(gT[t], bank[2][:]).then_inc(g_T, 1)
                        for t in range(2):
                            act.wait_ge(g_mm, j * 2 + t + 1)
                            nc.scalar.activation(gates[t], bank[4 if t == 0 else 6][:], ACT.Tanh, scale=0.5).then_inc(g_tanh, 1)
                        act.sem_inc(L1.agg_free, 1)
                        for t in range(2):
                            act.wait_ge(g_pre, j * 2 + t + 1)
                            nc.scalar.activation(gn[t], ga[t], ACT.Tanh).then_inc(g_n, 1)
                        act.wait_ge(x3_ready, j + 1)
                        pair = xs[:, ds(j * 2 * D, 2 * D)].rearrange("p (t f) -> p t f", t=2)
                        act.dma_start(x3_t[:, ds(j * 2, 2), :], pair).then_inc(x3_store, 16)
                        if isinstance(j, int) and j == NPAIR - 1:
                            act.dma_start(a["out"][j * 2 * P:j * 2 * P + P, :], xt(j * 2)).then_inc(x3_store, 16)
                            act.dma_start(a["out"][(NT - 1) * P:N, :], xt(NT - 1)[0:LAST, :]).then_inc(x3_store, 16)
                        else:
                            act.dma_start(a["out_t"][:, ds(j * 2, 2), :], pair).then_inc(x3_store, 16)

                layer1(0, True, False, False)
                layer1(1, True, True, False)
                with act.Fori(2, NPAIR) as i:
                    layer1(i, True, True, True)
                layer1(NPAIR, False, True, True)
                layer1(NPAIR + 1, False, False, True)
                act.wait_ge(x3_store, 16 * (2 * NPAIR + 1))
                act.sem_inc(x3_stored, 1)

                def copy_group(grp):
                    act.wait_ge(e_tr, grp + 1)
                    for k in range(KD):
                        last = copy(xT[:, k * 512:k * 512 + 512], bank[k][:])
                    last.then_inc(e_T, 1)

                act.wait_ge(be1_in, 16)
                copy_group(0)
                with act.Fori(0, NE1) as e:
                    for g in range(GROUPS):
                        grp = e * GROUPS + g
                        for c in range(KF):
                            hold(act, e_h, grp * KF + c + 1)
                            if c == 0:
                                hold(act, e_y, grp * 4)
                            nc.scalar.activation(hE[:, c * 512:c * 512 + 512], bank[2 + c % 3][:], ACT.Relu,
                                                 bias=be1[:, ds(e * KF + c, 1)]).then_inc(e_relu, 1)
                        if g < GROUPS - 1:
                            copy_group(grp + 1)
                        else:
                            with act.If(e < NE1 - 1):
                                copy_group(grp + 1)

            @block.tensor
            def _(pe):
                pe.wait_ge(cnt_made, 1)
                mm(bank[0][0:1, 0:NT], ones[0:FP, 0:1], ring[0:FP, 0:NT], True, True)
                mm(bank[0][0:1, 256:257], ones[:, 0:1], small[:, 16:17], True, True).then_inc(cnt_read, 1)

                pe.wait_ge(weights0_in, 16 * 11)
                with pe.Fori(0, NPAIR) as i:
                    pe.wait_ge(p_tn, i + 1)
                    pe.wait_ge(p_tT, i)
                    transposes(bank[2], [tn[:, 0:D], tn[:, D:2 * D]]).then_inc(p_tr, 1)
                    pe.wait_ge(p_tT, i + 1)
                    pe.wait_ge(p_out, i)
                    for t in range(2):
                        for k in range(KD):
                            last = mm(bank[3][:, t * D:t * D + D], tT[:, k * D + t * P:k * D + t * P + P],
                                      wg[:, k * D:k * D + D], k == 0, k == KD - 1)
                    last.then_inc(p_mm, 1)

                def transpose_pair(i):
                    pe.wait_ge(t_ready, i + 1)
                    transposes(bank[2], [tn[:, 0:D], tn[:, D:2 * D]]).then_inc(t_tr, 1)

                def logits0(i):
                    pe.wait_ge(tT_ready, i + 1)
                    for t in range(2):
                        for k in range(KD):
                            last = mm(bank[7][:, 8 * t:8 * t + 8], tT[:, k * D + t * P:k * D + t * P + P],
                                      rwT[:, 8 * k:8 * k + 8], k == 0, k == KD - 1)
                    last.then_inc(lg_ready, 1)

                def hidden(j, e):
                    pe.wait_ge(gelu_done, j * 8 + max(e - 1, 0))
                    for c in range(2):
                        for k in range(KD):
                            o = (2 * e + k) * D + c * P
                            last = mm(bank[3 + e % 2][:, c * D:c * D + D], w1_0[:, o:o + P],
                                      tT[:, k * D:k * D + D], k == 0, k == KD - 1)
                    last.then_inc(h_ready, 1)

                def second(j, item):
                    y = bank[5 + item % 2]
                    pe.wait_ge(acc_done, j * 9 + max(item - 1, 0))
                    if item < 8:
                        pe.wait_ge(gelu_done, j * 8 + item + 1)
                    else:
                        pe.wait_ge(combT_in, j + 1)
                    for t in range(2):
                        if item < 8:
                            for c in range(2):
                                o = (2 * item + c) * D
                                last = mm(y[:, t * D:t * D + D], hT[item % 2][:, c * D + t * P:c * D + t * P + P],
                                          w2_0[:, o:o + D], c == 0, c == 1)
                        else:
                            last = mm(y[:, t * D:t * D + D], combT[:, t * P:t * P + P], b2_0[:], True, True)
                    last.then_inc(mm2_done, 1)

                def layer0(i, inner, ffn):
                    if inner:
                        pe.wait_ge(L0.agg_free, i)
                        for t in range(2):
                            segment_sum(pe, L0, i * 2 + t, agg[t], D)
                    if ffn:
                        j = i - 1
                        hidden(j, 0)
                        for e in range(NE0):
                            if e < NE0 - 1:
                                hidden(j, e + 1)
                            else:
                                pe.wait_ge(comb_ready, j + 1)
                                for t in range(2):
                                    last = nc.tensor.transpose(bank[7][0:NE0, 128 + t * P:128 + t * P + P],
                                                               small[:, 64 + 8 * t:72 + 8 * t], ident[:])
                                last.then_inc(combT_tr, 1)
                                if inner:
                                    transpose_pair(i)
                            second(j, e)
                        second(j, 8)
                    elif inner:
                        transpose_pair(i)
                    if inner:
                        logits0(i)

                pe.wait_ge(sched_made, 2)
                pe.wait_ge(ring_clear, 1)
                layer0(0, True, False)
                with pe.Fori(1, NPAIR) as i:
                    layer0(i, True, True)
                layer0(NPAIR, False, True)

                pe.wait_ge(weights1_in, 48)
                for g, (lo, hi) in enumerate(((0, 2 * D), (2 * D, 3 * D))):
                    w = hi - lo
                    o = bank[3 + g]
                    mm(o[0:17, 0:w], e16[:], bih[:, lo:hi], True, False)
                    if g == 0:
                        mm(o[0:17, 0:w], e16[:], bhh[:, lo:hi], False, False)
                    for k in range(KD):
                        mm(o[0:17, 0:w], relT[:, 17 * k:17 * k + 17], wih[:, 3 * D * k + lo:3 * D * k + hi],
                           False, k == KD - 1)
                mm(bank[4][0:17, D:2 * D], e16[:], bhh[:, 2 * D:3 * D], True, True).then_inc(relw_mm, 1)
                pe.wait_ge(relw_in, 1)

                def gate_transposes(j, t):
                    pe.wait_ge(red_in, j * 2 + t + 1)
                    if t == 0:
                        pe.wait_ge(hin_in, j * 16 + 16)
                    pe.wait_ge(g_T, j * 2 + t)
                    for k in range(KD):
                        nc.tensor.transpose(bank[2][:, k * P:k * P + P], red[t][:, k * P:k * P + P], ident[:])
                        nc.tensor.transpose(bank[2][:, (2 + k) * P:(3 + k) * P], hin[:, t * D + k * P:t * D + k * P + P], ident[:])
                    nc.tensor.transpose(agg[t][0:17, 384:512], red[t][:, 256:273], ident[:]).then_inc(g_tr, 1)

                def gate_products(j, t):
                    pe.wait_ge(g_T, j * 2 + t + 1)
                    pe.wait_ge(g_n, j * 2)
                    rz, n_ = bank[4 if t == 0 else 6], bank[3 + 2 * t]
                    mm(rz[:], cT[t], relw[:, 0:512], True, False)
                    for k in range(KD):
                        mm(rz[:], gT[t][:, k * P:k * P + P], wih[:, 768 * k:768 * k + 512], False, False)
                        mm(rz[:], gT[t][:, 256 + k * P:256 + k * P + P], whh[:, 768 * k:768 * k + 512], False, k == 1)
                    mm(n_[:], cT[t], relw[:, 512:1024], True, False)
                    for k in range(KD):
                        mm(n_[:, 0:D], gT[t][:, k * P:k * P + P], wih[:, 768 * k + 512:768 * k + 768], False, False)
                        last = mm(n_[:, D:2 * D], gT[t][:, 256 + k * P:256 + k * P + P],
                                  whh[:, 768 * k + 512:768 * k + 768], False, k == 1)
                    last.then_inc(g_mm, 1)

                def logits1(k_):
                    pe.wait_ge(r_T, k_ + 1)
                    pe.wait_ge(r_done, k_)
                    for t in range(2):
                        for k in range(KD):
                            mm(bank[7][:, 8 * t:8 * t + 8], tT[:, k * D + t * P:k * D + t * P + P],
                               gateT[:, 8 * k:8 * k + 8], k == 0, False)
                        last = mm(bank[7][:, 8 * t:8 * t + 8], ones[0:1, :], gateb[:], False, True)
                    last.then_inc(r_lg, 1)

                def positions(k_):
                    pe.wait_ge(r_oh, k_ + 1)
                    for t in range(2):
                        o = bank[7][:, 16 + 8 * t:24 + 8 * t]
                        mm(o, ones[:], ohs[:, 16:24], True, False)
                        if t == 1:
                            mm(o, ones[:], ohs[:, 0:8], False, False)
                        last = mm(o, upper[:], ohs[:, 8 * t:8 * t + 8], False, True)
                    last.then_inc(r_pos, 1)

                def slots(k_):
                    pe.wait_ge(r_slot, k_ + 1)
                    for t in range(2):
                        last = mm(bank[7][:, 256:512], ohlo[t], ohhi[t], t == 0, t == 1)
                    last.then_inc(r_inv, 1)

                def layer1(i, inner, gru, route):
                    if inner:
                        pe.wait_ge(red_in, i * 2)
                        for t in range(2):
                            if t == 0:
                                pe.wait_ge(L1.agg_free, max(i - 1, 0) if isinstance(i, int) else i - 1)
                            segment_sum(pe, L1, i * 2 + t, agg[t], RW)
                    if route:
                        pe.wait_ge(r_t, i - 1)
                        pe.wait_ge(g_T, (i - 1) * 2)
                        transposes(bank[2], [tn[:, 0:D], tn[:, D:2 * D]]).then_inc(r_tr, 1)
                        pe.wait_ge(r_T, i - 1)
                        logits1(i - 2)
                    if gru:
                        for t in range(2):
                            gate_transposes(i - 1, t)
                        gate_products(i - 1, 0)
                    if route:
                        positions(i - 2)
                    if gru:
                        gate_products(i - 1, 1)
                    if route:
                        slots(i - 2)

                layer1(0, True, False, False)
                layer1(1, True, True, False)
                with pe.Fori(2, NPAIR) as i:
                    layer1(i, True, True, True)
                layer1(NPAIR, False, True, True)
                layer1(NPAIR + 1, False, False, True)

                def transpose_group(grp):
                    pe.wait_ge(e_norm, grp + 1)
                    pe.wait_ge(e_T, grp)
                    for k in range(KD):
                        for t in range(4):
                            last = nc.tensor.transpose(bank[k][:, t * P:t * P + P],
                                                       xn[:, t * D + k * P:t * D + k * P + P], ident[:])
                    last.then_inc(e_tr, 1)

                pe.wait_ge(e_consts, 1)
                transpose_group(0)
                with pe.Fori(0, NE1 // 2) as ep:
                    for be in range(2):
                        pe.wait_ge(we_in[be], ep * 48 + 48)
                        for g in range(GROUPS):
                            grp = (ep * 2 + be) * GROUPS + g
                            pe.wait_ge(e_T, grp + 1)
                            for c in range(KF):
                                if c >= 3:
                                    pe.wait_ge(e_relu, grp * KF + c - 2)
                                else:
                                    pe.wait_ge(e_relu, grp * KF)
                                for k in range(KD):
                                    last = mm(bank[2 + c % 3][:], we1[be][:, k * F1 + c * P:k * F1 + c * P + P],
                                              xT[:, k * 512:k * 512 + 512], k == 0, k == KD - 1)
                                last.then_inc(e_h, 1)
                            if be == 1 and g == GROUPS - 1:
                                with pe.If(ep < NE1 // 2 - 1):
                                    transpose_group(grp + 1)
                            else:
                                transpose_group(grp + 1)
                            pe.wait_ge(e_relu, grp * KF + KF)
                            pe.wait_ge(e_out, grp)
                            for t in range(4):
                                y = bank[5 + t // 2][:, (t % 2) * D:(t % 2) * D + D]
                                for c in range(KF):
                                    last = mm(y, hE[:, c * 512 + t * P:c * 512 + t * P + P],
                                              we2[be][:, c * D:c * D + D], c == 0, c == KF - 1)
                                last.then_inc(e_y, 1)
                        nc.tensor.matmul(bank[7][0:1, 0:1], ones[:, 0:1], we1[be][:, 0:1], start=True, stop=True,
                                         skip_group_check=True).then_inc(e_used, 1)


def kernel(x, src, dst, edge_type_16, edge_weight1, L0_gnn_weight, L0_gnn_bias, L0_ffn_router_w, L0_ffn_w1, L0_ffn_b1,
           L0_ffn_w2, L0_ffn_b2, L1_gnn_relvectors, L1_gnn_w_ih, L1_gnn_w_hh, L1_gnn_b_ih, L1_gnn_b_hh, L1_ffn_gate_w,
           L1_ffn_gate_b, L1_ffn_w1, L1_ffn_b1, L1_ffn_w2, L1_ffn_b2):
    import numpy as np
    import concourse.bacc as bacc
    from concourse.bass_utils import run_bass_kernel_spmd

    def tiles(v, fill):
        v = np.asarray(v).reshape(-1)
        return np.ascontiguousarray(np.pad(v, (0, EPAD - E), constant_values=fill).reshape(T, P).T)

    def split(w, k):
        w = np.asarray(w)
        return np.ascontiguousarray(w.reshape(k, P, -1).transpose(1, 0, 2).reshape(P, -1))

    c = np.ascontiguousarray
    relT = np.pad(np.asarray(L1_gnn_relvectors).T, ((0, 0), (0, 1)))
    flat = np.pad(np.asarray(dst), (0, EPAD + T - E), constant_values=FAR).reshape(P + 1, T)
    arrays = {
        "x": c(x),
        "src_tiles": tiles(src, 0), "dst_tiles": tiles(dst, FAR), "w_tiles": tiles(edge_weight1, 0),
        "rel_tiles": tiles(edge_type_16, 0),
        "dst_flat": flat[:P], "dst_next": c(flat[1:, 0:1]), "dst_firsts": c(flat.reshape(-1)[:EPAD:2 * P]).reshape(FP, FK),
        "wg": split(L0_gnn_weight, KD), "gbias": c(L0_gnn_bias),
        "rwT": split(np.asarray(L0_ffn_router_w).T, KD),
        "w1_0": c(np.asarray(L0_ffn_w1).reshape(NE0, 2, P, D).transpose(2, 0, 1, 3).reshape(P, -1)),
        "w2_0": c(np.asarray(L0_ffn_w2).reshape(NE0, 2, P, D).transpose(2, 0, 1, 3).reshape(P, -1)),
        "b1_0": c(np.asarray(L0_ffn_b1).reshape(NE0, 2, P).transpose(2, 0, 1).reshape(P, -1)),
        "b2_0": c(L0_ffn_b2),
        "relT": split(relT, KD),
        "w_ihT": split(np.asarray(L1_gnn_w_ih).T, KD), "w_hhT": split(np.asarray(L1_gnn_w_hh).T, KD),
        "b_ih": c(L1_gnn_b_ih).reshape(1, -1), "b_hh": c(L1_gnn_b_hh).reshape(1, -1),
        "gateT": split(L1_ffn_gate_w, KD), "gateb": c(L1_ffn_gate_b).reshape(1, -1),
        "w1_1": c(np.asarray(L1_ffn_w1).reshape(NE1, KD, P, F1).transpose(0, 2, 1, 3).reshape(NE1, P, -1)),
        "b1_1": c(np.asarray(L1_ffn_b1).reshape(NE1, KF, P).transpose(2, 0, 1).reshape(P, -1)),
        "w2_1": c(np.asarray(L1_ffn_w2).reshape(NE1, KF, P, D).transpose(0, 2, 1, 3).reshape(NE1, P, -1)),
        "b2_1": c(L1_ffn_b2),
    }
    nc = bacc.Bacc("TRN2", target_bir_lowering=False, num_devices=1)
    a = {n: nc.dram_tensor(n + "_in", v.shape, mybir.dt.from_np(v.dtype), kind="ExternalInput").ap()
         for n, v in arrays.items()}
    out = nc.dram_tensor("out", (N, D), mybir.dt.float32, kind="ExternalOutput").ap()
    a["out"] = out
    a["out_t"] = out[0:(NT - 1) * P, :].rearrange("(n p) f -> p n f", p=P)
    build(nc, a)
    r = run_bass_kernel_spmd(nc, [{n + "_in": v for n, v in arrays.items()}], core_ids=[0])
    return r.results[0]["out"]
```
